# Optimizing a Trainium2 kernel written in Bass

```python
import numpy as np
import jax
import jax.numpy as jnp

def _softmax(x, axis=-1):
    return jax.nn.softmax(x, axis=axis)

def _gelu(x):
    return jax.nn.gelu(x, approximate=True)

def _silu(x):
    return jax.nn.silu(x)

def _sigmoid(x):
    return jax.nn.sigmoid(x)

def _layernorm(x, axis=-1, eps=1e-05):
    m = jnp.mean(x, axis=axis, keepdims=True)
    v = jnp.var(x, axis=axis, keepdims=True)
    return (x - m) / jnp.sqrt(v + eps)

def _scatter_add(tgt, idx, src, axis=0):
    return tgt.at[idx].add(src)

def _segment_sum(src, seg, n):
    return jax.ops.segment_sum(src, seg, n)
kernel_name = 'mk_gnn_preln_d2_gnn_r8_8f2f3f'

def setup_inputs(seed: int=0):
    np.random.seed(seed)
    _w = jnp.asarray

    def _rec_inputs():
        import jax
        import jax.numpy as jnp
        _gk = jax.random.key(seed)
        x = -0.000202 + 1 * jax.random.normal(jax.random.fold_in(_gk, 1), (6250, 128), jnp.float32)
        src = jax.random.randint(jax.random.fold_in(_gk, 2), (100000,), 0, 6250, jnp.int32)
        dst = jax.random.randint(jax.random.fold_in(_gk, 3), (100000,), 0, 6250, jnp.int32)
        _o = jnp.argsort(dst, stable=True)
        src = src[_o]
        dst = dst[_o]
        edge_weight = jax.random.uniform(jax.random.fold_in(_gk, 12), (100000,), jnp.float32, 0.0, 0.999999)
        return (x, src, dst, edge_weight)
    x, src, dst, edge_weight = _rec_inputs()

    def _L0_gnn_setup():
        import jax, jax.numpy as jnp
        import numpy as np
        N_NODES = 6250
        N_EDGES = 75000
        IN_DIM = 128
        OUT_DIM = 128
        key = jax.random.key(seed)
        k1, k2, k3, k4, k5, k6 = jax.random.split(key, 6)
        batch_x = jax.random.normal(k1, (N_NODES, IN_DIM), dtype=jnp.float32)
        edge_src = jax.random.randint(k2, (N_EDGES,), 0, N_NODES, dtype=jnp.int32)
        edge_dst = jax.random.randint(k3, (N_EDGES,), 0, N_NODES, dtype=jnp.int32)
        edge_weight = jax.random.uniform(k4, (N_EDGES,), dtype=jnp.float32)
        stdv = 1.0 / np.sqrt(OUT_DIM)
        weight = jax.random.uniform(k5, (IN_DIM, OUT_DIM), dtype=jnp.float32, minval=-stdv, maxval=stdv)
        bias = jax.random.uniform(k6, (OUT_DIM,), dtype=jnp.float32, minval=-stdv, maxval=stdv)
        return {'batch_x': batch_x, 'edge_weight': edge_weight, 'weight': weight, 'bias': bias, 'edge_src': edge_src, 'edge_dst': edge_dst}
    _L0_gnn_all = _L0_gnn_setup()
    _L0_gnn_in = {k: v for k, v in _L0_gnn_all.items() if k in ('weight', 'bias')}
    del _L0_gnn_all

    def _L1_gnn_setup():
        import jax, jax.numpy as jnp
        import numpy as np
        N_NODES = 6250
        N_EDGES = 100000
        IN_DIM = 128
        OUT_DIM = 128
        DELTA = 0.5
        key = jax.random.key(seed)
        k1, k2, k3, k4, k5, k6 = jax.random.split(key, 6)
        node_feat = jax.random.normal(k1, (N_NODES, IN_DIM), dtype=jnp.float32)
        dist = jax.random.uniform(k2, (N_EDGES,), dtype=jnp.float32)
        src = jax.random.randint(k3, (N_EDGES,), 0, N_NODES)
        dst = jax.random.randint(k4, (N_EDGES,), 0, N_NODES)
        edge_w = jax.random.normal(k5, (2 * IN_DIM + 1, OUT_DIM), dtype=jnp.float32) * 0.05
        node_w = jax.random.normal(k6, (IN_DIM + OUT_DIM, OUT_DIM), dtype=jnp.float32) * 0.05
        return {'node_feat': node_feat, 'dist': dist, 'src': src, 'dst': dst, 'edge_w': edge_w, 'node_w': node_w}
    _L1_gnn_all = _L1_gnn_setup()
    _L1_gnn_in = {k: v for k, v in _L1_gnn_all.items() if k in ('edge_w', 'node_w')}
    del _L1_gnn_all
    return {'x': x, 'src': src, 'dst': dst, 'edge_weight': edge_weight, 'L0_gnn_weight': _L0_gnn_in['weight'], 'L0_gnn_bias': _L0_gnn_in['bias'], 'L1_gnn_edge_w': _L1_gnn_in['edge_w'], 'L1_gnn_node_w': _L1_gnn_in['node_w']}

def reference(x, src, dst, edge_weight, L0_gnn_weight, L0_gnn_bias, L1_gnn_edge_w, L1_gnn_node_w):
    import jax
    import jax.numpy as jnp

    def _L0_gnn_ref(batch_x, edge_weight, weight, bias, edge_src, edge_dst):
        import jax, jax.numpy as jnp
        import numpy as np
        N_NODES = 6250
        N_EDGES = 75000
        IN_DIM = 128
        OUT_DIM = 128
        msgs = batch_x[edge_src] * edge_weight[:, None]
        agg = jax.ops.segment_sum(msgs, edge_dst, num_segments=N_NODES)
        return agg @ weight + bias

    def _L1_gnn_ref(node_feat, dist, src, dst, edge_w, node_w):
        import jax, jax.numpy as jnp
        import numpy as np
        N_NODES = 6250
        N_EDGES = 100000
        IN_DIM = 128
        OUT_DIM = 128
        DELTA = 0.5
        u = node_feat[src]
        v = node_feat[dst]
        feat = jnp.concatenate([u, dist[:, None], v], axis=-1)
        msg = jax.nn.leaky_relu(feat @ edge_w, negative_slope=0.01)
        mask = (dist < DELTA)[:, None].astype(msg.dtype)
        masked_msg = msg * mask
        aggr = jax.ops.segment_sum(masked_msg, dst, num_segments=N_NODES)
        h = jnp.concatenate([node_feat, aggr], axis=-1)
        return jax.nn.leaky_relu(h @ node_w, negative_slope=0.01)
    h = jnp.maximum(_layernorm(x, axis=-1), 0.0)
    x = x + _L0_gnn_ref(h, edge_weight, L0_gnn_weight, L0_gnn_bias, src, dst)
    h = jnp.maximum(_layernorm(x, axis=-1), 0.0)
    x = x + _L1_gnn_ref(h, edge_weight, src, dst, L1_gnn_edge_w, L1_gnn_node_w)
    return x

_drawn_inputs = setup_inputs


def setup_inputs(seed=0):
    import zlib

    import numpy as np

    out = dict(_drawn_inputs(seed))
    spreads = {}
    factors = {}
    for name, (base, spread) in spreads.items():
        noise = np.random.default_rng([zlib.crc32(name.encode()), seed]).standard_normal(out[name].shape)
        drawn = base * np.exp(spread * noise) if base else spread * noise
        out[name] = jnp.asarray(drawn.astype(out[name].dtype))
    for name, factor in factors.items():
        out[name] = (out[name] * factor).astype(out[name].dtype)
    return out
```

```python
from contextlib import ExitStack

import concourse.bass as bass
from concourse import mybir

P = 128
N_NODES = 6250
N_EDGES = 100000
D = 128
EPS = 1e-5
DELTA = 0.5
SLOPE = 0.01

TPC = 4
SLOTS = 4
CHUNKS = -(-N_EDGES // (P * TPC * SLOTS)) * SLOTS
TILES = CHUNKS * TPC
ROUNDS = CHUNKS // SLOTS
CE = P * TPC
NT = -(-N_NODES // P)
NP = NT * P
GT = 7
GROUPS = NT // GT
GW = GT * P
LAST = N_NODES - (NT - 1) * P
W0 = 64
W1 = 96
NPAD = NP + P
CH2 = CHUNKS // 2
ROUND_MAGIC = 8388608.0
FAR = 16384.0

ALU = mybir.AluOpType
ACT = mybir.ActivationFunctionType
F32 = mybir.dt.float32
I32 = mybir.dt.int32
AX_X = mybir.AxisListType.X


def gnn_kernel(nc, x, src_t, dst_t, w_t, dst_row, w_row, w0, b0, edge_w, node_w, out):
    ctx = ExitStack()
    with ctx:
        def sb(name, shape, dt=F32):
            return ctx.enter_context(nc.sbuf_tensor(name, shape, dt))

        def pb(name, shape):
            return ctx.enter_context(nc.psum_tensor(name, shape, F32))

        def sem(name):
            return ctx.enter_context(nc.semaphore(name))

        def slot_sems(name):
            return [sem(f"{name}{s}") for s in range(SLOTS)]

        h_rows = nc.dram_tensor("h_rows", (NP, D), F32).ap()
        u_rows = nc.dram_tensor("u_rows", (NP, D), F32).ap()
        v_rows = nc.dram_tensor("v_rows", (NPAD, D), F32).ap()

        xs = sb("xs", [P, NT * D])
        hs = sb("hs", [P, NT * D])
        root = sb("root", [P, NT * D])
        accT = sb("accT", [P, NPAD])
        srcs = sb("srcs", [P, TILES + SLOTS * TPC], I32)
        dsti = sb("dsti", [P, TILES], I32)
        wts = sb("wts", [P, TILES])
        dstf = sb("dstf", [P, TILES])
        rel0 = sb("rel0", [P, TILES])
        rel1 = sb("rel1", [P, TILES])
        cmin = sb("cmin", [P, 2, CHUNKS])
        crow = sb("crow", [CH2, 2, 2])
        qcol = sb("qcol", [CH2, 2, 4])
        crep = sb("crep", [CH2, 2, 3, P])
        cbase = sb("cbase", [P, 3, CHUNKS])
        xbef = sb("xbef", [P, 2, CHUNKS])
        zeros = sb("zeros", [P, CHUNKS])
        meta = sb("meta", [1, 2, CHUNKS * 4], I32)
        pbase = sb("pbase", [P, CHUNKS])
        iota_c = sb("iota_c", [P, P])
        shift = sb("shift", [P, 2, NPAD // W0 + 1])
        iota_p = sb("iota_p", [P, 1])
        ident = sb("ident", [P, P])
        w0s = sb("w0s", [P, D])
        bias = sb("bias", [P, D])
        wuvr = sb("wuvr", [P, 3, D])
        wn2 = sb("wn2", [P, D])
        st = sb("st", [P, GT, 6])
        mv = sb("mv", [P, GT, 2])
        ve = sb("ve", [P, GT])
        sd = sb("sd", [P, GT])
        rstd = sb("rstd", [P, NT])
        nmr = sb("nmr", [P, NT])
        idx = sb("idx", [P, SLOTS, TPC], I32)
        G = sb("G", [P, SLOTS, TPC, D])
        OH = sb("OH", [P, SLOTS, TPC, W1])
        OHT = sb("OHT", [W1 + 1, SLOTS, CE])
        VW = sb("VW", [W1 + 1, SLOTS, D])
        DB = sb("DB", [W1, SLOTS, CE], I32)
        M = sb("M", [P, SLOTS, TPC * D])
        OHx = sb("OHx", [P, TPC, W1])
        OHTx = sb("OHTx", [W1 + 1, CE])
        VWx = sb("VWx", [W1 + 1, D])
        DBx = sb("DBx", [W1, CE], I32)
        relx = sb("relx", [P, TPC])
        pbx = sb("pbx", [P, 1])
        agg = sb("agg", [P, GW])
        h2 = sb("h2", [P, GW])
        h2T = sb("h2T", [P, GW])
        uv = sb("uv", [P, 2, GT, D])
        ob = sb("ob", [P, GW])

        ps = [pb(f"ps{b}", [P, 512]) for b in range(8)]
        PRE, ACC = ps[0:4], ps[4:8]

        s_x = [sem("s_xin0"), sem("s_xin1")]
        s_edges, s_weights, s_iota, s_const = sem("s_edges"), sem("s_weights"), sem("s_iota"), sem("s_const")
        s_dve = sem("s_dve")
        s_st, s_mv, s_rs = sem("s_st"), sem("s_mv"), sem("s_rs")
        s_var, s_std, s_rstd, s_h, s_hrows = sem("s_var"), sem("s_std"), sem("s_rstd"), sem("s_h"), sem("s_hrows")
        s_cmin, s_cminT, s_crep, s_cb, s_meta = sem("s_cmin"), sem("s_cminT"), sem("s_crep"), sem("s_cb"), sem("s_meta")
        s_vpad = sem("s_vpad")
        s_tick = {e.engine: sem(f"s_tick_{e.engine.name}") for e in (nc.gpsimd, nc.vector, nc.scalar, nc.sync)}
        A_idx, A_g, A_oh, A_mm, A_acc = (slot_sems(n) for n in ("A_idx", "A_g", "A_oh", "A_mm", "A_acc"))
        Ax_rel, Ax_oh, Ax_mm, Ax_acc = sem("Ax_rel"), sem("Ax_oh"), sem("Ax_mm"), sem("Ax_acc")
        B_idx, B_g, B_in, B_oh, B_pre, B_add, B_low, B_msg, B_mm, B_acc = (
            slot_sems(n) for n in ("B_idx", "B_g", "B_in", "B_oh", "B_pre", "B_add", "B_low", "B_msg", "B_mm", "B_acc"))
        Bx_in, Bx_rel, Bx_oh, Bx_pre, Bx_add, Bx_low, Bx_msg, Bx_mm, Bx_acc = (
            sem(n) for n in ("Bx_in", "Bx_rel", "Bx_oh", "Bx_pre", "Bx_add", "Bx_low", "Bx_msg", "Bx_mm", "Bx_acc"))
        s_agg, s_y, s_x1, s_h2, s_h2t, s_h2T, s_uvr, s_uv, s_root, s_urows, s_uvfree = (
            sem(n) for n in ("s_agg", "s_y", "s_x1", "s_h2", "s_h2t", "s_h2T", "s_uvr", "s_uv", "s_root", "s_urows", "s_uvfree"))
        s_acc0, s_acc1 = sem("s_acc0"), sem("s_acc1")
        f_agg, f_z, f_sum, f_low, f_max, f_out, s_stored = (
            sem(n) for n in ("f_agg", "f_z", "f_sum", "f_low", "f_max", "f_out", "s_stored"))

        block = ctx.enter_context(nc.Block())

        def rows(dram, g):
            return dram[bass.ds(g * GW, GW), :].rearrange("(t p) d -> p t d", p=P)

        def cols(sbuf, g):
            return sbuf[:, bass.ds(g * GW, GW)]

        TAKERS = {nc.scalar: range(0, GT, 2), nc.vector: range(1, GT, 2)}

        def taken(eng, g, j):
            mine = TAKERS[eng]
            return (g + 1) * len(mine) + (j - mine[0]) // 2 + 1

        def take_uvr(eng, copy, g, j, semaphore):
            eng.wait_ge(s_uvr, g * GT + j + 2)
            if j == TAKERS[eng][0]:
                eng.wait_ge(s_uvfree, g + 1)
            bank = ps[4 + j % 4]
            copy(root[:, bass.ds((g * GT + j) * D, D)], bank[:, 2 * D:3 * D])
            copy(uv[:, :, j, :], bank[:, 0:2 * D].rearrange("p (k d) -> p k d", k=2)).then_inc(semaphore, 1)

        def hold(eng, semaphore, value):
            eng.wait_ge(semaphore, value)
            eng.sem_inc(s_tick[eng.engine], 1)

        def window_start(base, k, w):
            return nc.s_assert_within(base + k * w, w, N_NODES,
                                      skip_runtime_bounds_check_because="a chunk's last window starts at its greatest dst at most")

        def extra_windows(eng, nx, before, body):
            with eng.If(nx > 0):
                with eng.Fori(1, nx + 1) as k:
                    body(k, before + k)

        def load_meta(eng, layer, c):
            def get(k, top):
                return eng.value_load(meta[0:1, layer, bass.ds(c * 4 + k, 1)], min_val=0, max_val=top)
            return get(0, N_NODES), get(1, N_NODES // W0), get(2, CHUNKS * P)

        @block.sync
        def _(sp):
            sp.sem_inc(s_uvfree, 1)
            half = (GROUPS // 2) * GT
            xr = x.rearrange("(t p) d -> p t d", p=P)
            xv = xs[:, :].rearrange("p (t d) -> p t d", d=D)
            sp.dma_start(xv[:, 0:half, :], xr[:, 0:half, :]).then_inc(s_x[0], 16)
            sp.dma_start(xv[:, half:NT, :], xr[:, half:NT, :]).then_inc(s_x[1], 16)
            sp.dma_start(srcs[:, 0:TILES], src_t).then_inc(s_edges, 16)
            sp.dma_start(dsti[:, :], dst_t).then_inc(s_edges, 16)
            sp.dma_start(wts[:, :], w_t).then_inc(s_edges, 16)
            sp.dma_start(w0s[:, :], w0).then_inc(s_weights, 16)
            sp.dma_start(bias[:, :], b0.partition_broadcast(P)).then_inc(s_weights, 16)
            sp.dma_start(wuvr[:, 0, :], edge_w[0:D, :]).then_inc(s_weights, 16)
            sp.dma_start(wuvr[:, 1, :], edge_w[D + 1:2 * D + 1, :]).then_inc(s_weights, 16)
            sp.dma_start(wuvr[:, 2, :], node_w[0:D, :]).then_inc(s_weights, 16)
            sp.dma_start(wn2[:, :], node_w[D:2 * D, :]).then_inc(s_weights, 16)
            for s in range(SLOTS):
                sp.dma_start(VW[W1:W1 + 1, s, :], edge_w[D:D + 1, :]).then_inc(s_weights, 16)
            sp.dma_start(VWx[W1:W1 + 1, :], edge_w[D:D + 1, :]).then_inc(s_weights, 16)
            with sp.Fori(0, GROUPS) as g:
                sp.wait_ge(s_h, g + 1)
                sp.dma_start(rows(h_rows, g), cols(hs, g).rearrange("p (t d) -> p t d", d=D)).then_inc(s_hrows, 16)
            sp.wait_ge(s_const, 1)
            sp.dma_start(v_rows[NP:NPAD, :], zeros[:, 0:D]).then_inc(s_vpad, 16)
            with sp.Fori(0, GROUPS) as g:
                sp.wait_ge(s_uv, taken(nc.scalar, g, GT - 1))
                sp.wait_ge(s_root, taken(nc.vector, g, GT - 2))
                sp.dma_start(rows(u_rows, g), uv[:, 0, :, :]).then_inc(s_urows, 16)
                sp.dma_start(rows(v_rows, g), uv[:, 1, :, :]).then_inc(s_urows, 16)
                sp.wait_ge(s_urows, 32 * (g + 1))
                sp.sem_inc(s_uvfree, 1)
            sp.wait_ge(s_vpad, 16)
            sp.wait_ge(s_urows, 32 * GROUPS)
            with sp.Fori(0, ROUNDS) as r:
                for s in range(SLOTS):
                    c = r * SLOTS + s
                    base = sp.value_load(meta[0:1, 1, bass.ds(c * 4, 1)], min_val=0, max_val=N_NODES)
                    sp.wait_ge(B_oh[s], r + 1)
                    sp.dma_start(DB[:, s, :], dst_row[0:1, bass.ds(c * CE, CE)].broadcast_to([W1, CE])).then_inc(B_in[s], 16)
                    sp.wait_ge(B_pre[s], r + 1)
                    sp.dma_start(VW[0:W1, s, :], v_rows[bass.ds(base, W1), :]).then_inc(B_in[s], 16)
                    sp.dma_start(OHT[W1:W1 + 1, s, :], w_row[0:1, bass.ds(c * CE, CE)]).then_inc(B_in[s], 16)
                for s in range(SLOTS):
                    c = r * SLOTS + s
                    base, nx, before = load_meta(sp, 1, c)
                    with sp.If(nx > 0):
                        with sp.Fori(1, nx + 1) as k:
                            sp.wait_ge(Bx_acc, before + k)
                            sp.dma_start(VWx[0:W1, :], v_rows[bass.ds(window_start(base, k, W1), W1), :]).then_inc(Bx_in, 16)
                            sp.dma_start(DBx[:, :], dst_row[0:1, bass.ds(c * CE, CE)].broadcast_to([W1, CE])).then_inc(Bx_in, 16)
                            sp.dma_start(OHTx[W1:W1 + 1, :], w_row[0:1, bass.ds(c * CE, CE)]).then_inc(Bx_in, 16)
            for g in range(GROUPS - 1):
                sp.wait_ge(f_out, g + 1)
                sp.dma_start(out[g * GW:(g + 1) * GW, :].rearrange("(t p) d -> p t d", p=P),
                             xs[:, g * GW:(g + 1) * GW].rearrange("p (t d) -> p t d", d=D)).then_inc(s_stored, 16)
            g = GROUPS - 1
            sp.wait_ge(f_out, g + 1)
            sp.dma_start(out[g * GW:(NT - 1) * P, :].rearrange("(t p) d -> p t d", p=P),
                         xs[:, g * GW:(NT - 1) * P].rearrange("p (t d) -> p t d", d=D)).then_inc(s_stored, 16)
            sp.dma_start(out[(NT - 1) * P:N_NODES, :], xs[0:LAST, (NT - 1) * P:NT * P]).then_inc(s_stored, 16)
            sp.wait_ge(s_stored, 16 * (GROUPS + 1))

        @block.gpsimd
        def _(pool):
            nc.gpsimd.iota(iota_c[:, :], [[1, P]], base=0, channel_multiplier=0,
                           allow_small_or_imprecise_dtypes=True).then_inc(s_iota, 1)
            nc.gpsimd.iota(iota_p[:, :], [[0, 1]], base=0, channel_multiplier=1,
                           allow_small_or_imprecise_dtypes=True).then_inc(s_iota, 1)
            for l, w in enumerate((W0, W1)):
                nc.gpsimd.iota(shift[:, l, :], [[w, NPAD // W0 + 1]], base=0, channel_multiplier=0,
                               allow_small_or_imprecise_dtypes=True).then_inc(s_iota, 1)

            def gathers(table, ready, landed):
                with pool.Fori(0, ROUNDS) as r:
                    for s in range(SLOTS):
                        hold(pool, ready[s], r + 1)
                        for j in range(TPC):
                            nc.gpsimd.indirect_dma_start(
                                out=G[:, s, j, :], out_offset=None, in_=table,
                                in_offset=bass.IndirectOffsetOnAxis(ap=idx[:, s, j:j + 1], axis=0)).then_inc(landed[s], 16)

            pool.wait_ge(s_hrows, 16 * GROUPS)
            gathers(h_rows, A_idx, A_g)
            pool.wait_ge(s_urows, 32 * GROUPS)
            gathers(u_rows, B_idx, B_g)

            with pool.Fori(0, GROUPS) as g:
                pool.wait_ge(f_max, g + 2)
                nc.gpsimd.tensor_tensor(cols(xs, g), cols(xs, g), cols(root, g), ALU.add).then_inc(f_out, 1)

        @block.scalar
        def _(act):
            act.sem_inc(s_h2T, 1)
            act.sem_inc(s_uv, len(TAKERS[nc.scalar]))
            def ln_group(g, count, dest):
                act.wait_ge(s_var, count)
                nc.scalar.activation(sd[:, :], ve[:, :], ACT.Sqrt).then_inc(s_std, 1)
                act.wait_ge(s_rstd, count)
                for j in range(GT):
                    t = g * GT + j
                    last = nc.scalar.activation(dest(j), xs[:, bass.ds(t * D, D)], ACT.Relu,
                                                bias=nmr[:, bass.ds(t, 1)], scale=rstd[:, bass.ds(t, 1)])
                return last

            with act.Fori(0, GROUPS) as g:
                ln_group(g, g + 1, lambda j: hs[:, bass.ds((g * GT + j) * D, D)]).then_inc(s_h, 1)

            def copy_indices(r, s, free, ready):
                act.wait_ge(free[s], r + 1)
                nc.scalar.copy(idx[:, s, :], srcs[:, bass.ds((r * SLOTS + s) * TPC, TPC)]).then_inc(ready[s], 1)

            act.wait_ge(s_edges, 48)
            with act.Fori(0, ROUNDS) as r:
                for s in range(SLOTS):
                    copy_indices(r, s, A_mm, A_idx)

            def take_agg(g):
                act.wait_ge(s_y, g + 1)
                nc.scalar.copy(agg[:, :], cols(accT, g)).then_inc(s_agg, 1)

            def ln2(g):
                act.wait_ge(s_h2t, g + 1)
                ln_group(g, g + 1 + GROUPS, lambda j: h2[:, j * D:(j + 1) * D]).then_inc(s_h2, 1)

            def take_h2T(g):
                act.wait_ge(s_h2t, g + 2)
                act.wait_ge(s_uvr, g * GT + 1)
                nc.scalar.copy(h2T[:, 0:512], ps[2][:, 0:512])
                nc.scalar.copy(h2T[:, 512:GW], ps[3][:, 0:GW - 512]).then_inc(s_h2T, 1)

            def take_uv(g, tiles):
                for j in tiles:
                    if j in TAKERS[nc.scalar]:
                        take_uvr(act, nc.scalar.copy, g, j, s_uv)

            act.wait_ge(s_acc0, 1)
            take_agg(0)
            ln2(0)
            with act.Fori(0, GROUPS - 1) as g:
                take_agg(g + 1)
                take_h2T(g)
                take_uv(g, range(0, 3))
                ln2(g + 1)
                take_uv(g, range(3, GT))
            take_h2T(GROUPS - 1)
            take_uv(GROUPS - 1, range(GT))

            for s in range(SLOTS):
                copy_indices(0, s, B_add, B_idx)

            def low_side(s):
                return nc.scalar.mul(M[:, s, :], PRE[s][:, :], SLOPE)

            with act.Fori(0, ROUNDS) as r:
                for s in range(SLOTS):
                    _, nx, before = load_meta(act, 1, r * SLOTS + s)

                    def extra(k, n):
                        act.wait_ge(Bx_add, n)
                        low_side(s).then_inc(Bx_low, 1)
                    extra_windows(act, nx, before, extra)
                    act.wait_ge(B_add[s], r + 2)
                    low_side(s).then_inc(B_low[s], 1)
                    copy_indices(r + 1, s, B_add, B_idx)

            act.wait_ge(s_acc1, 1)
            with act.Fori(0, GROUPS) as g:
                act.wait_ge(f_z, g + 1)
                nc.scalar.copy(agg[:, :], cols(accT, g)).then_inc(f_agg, 1)
                act.wait_ge(f_sum, g + 1)
                nc.scalar.mul(root[:, bass.ds(g * GW, 512)], ps[0][:, :], SLOPE)
                nc.scalar.mul(root[:, bass.ds(g * GW + 512, GW - 512)], ps[1][:, 0:GW - 512], SLOPE).then_inc(f_low, 1)

        @block.vector
        def _(dve):
            done = [0]

            def after(ins):
                done[0] += 1
                ins.then_inc(s_dve, 1)
                dve.wait_ge(s_dve, done[0])

            for s in range(SLOTS):
                for primed in (A_acc[s], B_oh[s], B_add[s], B_msg[s], B_acc[s]):
                    dve.sem_inc(primed, 1)
            for primed in (s_x1, Ax_acc, Bx_acc, f_max):
                dve.sem_inc(primed, 1)
            dve.sem_inc(s_root, len(TAKERS[nc.vector]))
            nc.vector.memset(srcs[:, TILES:], 0)
            nc.vector.memset(zeros[:, :], 0.0).then_inc(s_const, 1)

            def ln_group(g, count):
                for j in range(GT):
                    last = nc.vector.bn_stats(st[:, j, :], xs[:, bass.ds((g * GT + j) * D, D)])
                last.then_inc(s_st, 1)
                hold(dve, s_st, count)
                for j in range(GT):
                    last = nc.vector.bn_aggr(mv[:, j, :], st[:, j, :])
                last.then_inc(s_mv, 1)
                dve.wait_ge(s_mv, count)
                nc.vector.tensor_scalar(ve[:, :], mv[:, :, 1], EPS, None, ALU.add).then_inc(s_var, 1)
                dve.wait_ge(s_std, count)
                nc.vector.reciprocal(rstd[:, bass.ds(g * GT, GT)], sd[:, :]).then_inc(s_rs, 1)
                dve.wait_ge(s_rs, count)
                nc.vector.scalar_tensor_tensor(out=nmr[:, bass.ds(g * GT, GT)], in0=mv[:, :, 0], scalar=-1.0,
                                               in1=rstd[:, bass.ds(g * GT, GT)], op0=ALU.mult, op1=ALU.mult).then_inc(s_rstd, 1)

            dve.wait_ge(s_x[0], 16)
            with dve.Fori(0, GROUPS // 2) as g:
                ln_group(g, g + 1)
            dve.wait_ge(s_x[1], 16)
            with dve.Fori(GROUPS // 2, GROUPS) as g:
                ln_group(g, g + 1)

            dve.wait_ge(s_iota, 4)
            nc.vector.tensor_scalar(ident[:, :], iota_c[:, :], iota_p[:, 0:1], None, ALU.is_equal).then_inc(s_const, 1)
            dve.wait_ge(s_edges, 48)
            after(nc.vector.tensor_copy(dstf[:, :], dsti[:, :]))
            chunked = dstf[:, :].rearrange("p (c t) -> p c t", t=TPC)
            nc.vector.tensor_reduce(cmin[:, 0, :], chunked, AX_X, ALU.min)
            nc.vector.tensor_reduce(cmin[:, 1, :], chunked, AX_X, ALU.max).then_inc(s_cmin, 1)
            dve.wait_ge(s_cminT, 1)
            for h in range(2):
                for m, op in enumerate((ALU.min, ALU.max)):
                    last = nc.vector.tensor_reduce(crow[:, h, m:m + 1], ps[2 * h + m][0:CH2, 0:P], AX_X, op)
            after(last)
            nc.vector.tensor_copy(qcol[:, :, 0], crow[:, :, 0])
            after(nc.vector.tensor_tensor(qcol[:, :, 3], crow[:, :, 1], crow[:, :, 0], ALU.subtract))
            for l, w in enumerate((W0, W1)):
                last = nc.vector.tensor_scalar(qcol[:, :, 1 + l], qcol[:, :, 3], 1.0 / w, 0.5 / w - 0.5, ALU.mult, ALU.add)
            after(last)
            after(nc.vector.tensor_scalar(qcol[:, :, 1:3], qcol[:, :, 1:3], ROUND_MAGIC, None, ALU.add))
            after(nc.vector.tensor_scalar(qcol[:, :, 1:3], qcol[:, :, 1:3], -ROUND_MAGIC, None, ALU.add))
            for h in range(2):
                for m in range(3):
                    last = nc.vector.tensor_scalar(crep[:, h, m, :], zeros[0:CH2, 0:P], qcol[:, h, m:m + 1], None, ALU.add)
            last.then_inc(s_crep, 1)
            dve.wait_ge(s_cb, 1)
            for h in range(2):
                last = nc.vector.tensor_copy(cbase[:, :, h * CH2:(h + 1) * CH2],
                                             ps[4 + h][:, 0:3 * P].rearrange("p (m c) -> p m c", m=3)[:, :, 0:CH2])
            after(last)
            for l in range(2):
                last = nc.vector.tensor_tensor_scan(xbef[:, l, :], cbase[:, 1 + l, :], zeros[:, :], 0.0, ALU.add, ALU.add)
            after(last)
            mrow = meta[0:1, :, :].rearrange("p l (c k) -> p l c k", k=4)
            for l in range(2):
                nc.vector.tensor_copy(mrow[:, l, :, 0], cbase[0:1, 0, :])
                nc.vector.tensor_copy(mrow[:, l, :, 1], cbase[0:1, 1 + l, :])
                last = nc.vector.tensor_tensor(mrow[:, l, :, 2], xbef[0:1, l, :], cbase[0:1, 1 + l, :], ALU.subtract)
            last.then_inc(s_meta, 1)
            spread = cbase[:, 0, :].rearrange("p (c o) -> p c o", o=1).broadcast_to([P, CHUNKS, TPC])
            after(nc.vector.tensor_tensor(rel0[:, :].rearrange("p (c t) -> p c t", t=TPC), chunked, spread, ALU.subtract))
            nc.vector.tensor_scalar(pbase[:, :], cbase[:, 0, :], iota_p[:, 0:1], None, ALU.add)
            after(nc.vector.tensor_scalar(rel1[:, :], wts[:, :], DELTA, FAR, ALU.is_ge, ALU.mult))
            nc.vector.tensor_tensor(rel1[:, :], rel1[:, :], rel0[:, :], ALU.add)
            after(nc.vector.memset(accT[:, :], 0.0))
            dve.wait_ge(s_meta, 1)

            def add_window(start, w, products):
                window = accT[:, bass.ds(start, w)]
                return nc.vector.tensor_tensor(window, window, products[:, 0:w], ALU.add)

            def weighted_onehots(dest, rel, c):
                for j in range(TPC):
                    last = nc.vector.tensor_scalar(dest[:, j, 0:W0], iota_c[:, 0:W0], rel(j),
                                                   wts[:, bass.ds(c * TPC + j, 1)], ALU.is_equal, ALU.mult)
                return last

            with dve.Fori(0, ROUNDS) as r:
                for s in range(SLOTS):
                    c = r * SLOTS + s
                    weighted_onehots(OH[:, s], lambda j: rel0[:, bass.ds(c * TPC + j, 1)], c).then_inc(A_oh[s], 1)
                for s in range(SLOTS):
                    c = r * SLOTS + s
                    hold(dve, A_acc[s - 1], r + (2 if s else 1))
                    base, nx, before = load_meta(dve, 0, c)

                    def extra(k, n):
                        nc.vector.tensor_scalar(relx[:, :], rel0[:, bass.ds(c * TPC, TPC)], shift[:, 0, bass.ds(k, 1)],
                                                None, ALU.subtract).then_inc(Ax_rel, 1)
                        dve.wait_ge(Ax_rel, n)
                        weighted_onehots(OHx, lambda j: relx[:, j:j + 1], c).then_inc(Ax_oh, 1)
                        dve.wait_ge(Ax_mm, n)
                        dve.wait_ge(Ax_acc, n)
                        add_window(window_start(base, k, W0), W0, ACC[s]).then_inc(Ax_acc, 1)
                    extra_windows(dve, nx, before, extra)
                    dve.wait_ge(Ax_acc, before + nx + 1)
                    dve.wait_ge(A_mm[s], r + 2)
                    add_window(base, W0, ACC[s]).then_inc(A_acc[s], 1)
            dve.wait_ge(A_acc[SLOTS - 1], ROUNDS + 1)
            dve.sem_inc(s_acc0, 1)

            dve.wait_ge(s_weights, 16 * (7 + SLOTS))
            biased = bias[:, :].rearrange("p (o d) -> p o d", o=1).broadcast_to([P, NT, D])
            xv = xs[:, :].rearrange("p (t d) -> p t d", d=D)
            after(nc.vector.tensor_tensor(xv, xv, biased, ALU.add))

            def x1_group(g):
                dve.wait_ge(s_y, g + 2)
                a, b = xs[:, bass.ds(g * GW, 512)], xs[:, bass.ds(g * GW + 512, GW - 512)]
                nc.vector.tensor_tensor(a, a, ps[0][:, 0:512], ALU.add)
                nc.vector.tensor_tensor(b, b, ps[1][:, 0:GW - 512], ALU.add).then_inc(s_x1, 1)
                dve.wait_ge(s_x1, g + 2)
                ln_group(g, g + 1 + GROUPS)

            def root_group(g):
                for j in TAKERS[nc.vector]:
                    take_uvr(dve, nc.vector.tensor_copy, g, j, s_root)

            x1_group(0)
            with dve.Fori(0, GROUPS - 1) as g:
                x1_group(g + 1)
                root_group(g)
            root_group(GROUPS - 1)

            after(nc.vector.memset(accT[:, :], 0.0))

            def onehots(dest, rel):
                for j in range(TPC):
                    last = nc.vector.tensor_scalar(dest[:, j, :], iota_c[:, 0:W1], rel(j), None, ALU.is_equal)
                return last

            def add_u(s):
                return nc.vector.tensor_tensor(PRE[s][:, :], G[:, s].rearrange("p t d -> p (t d)"), PRE[s][:, :], ALU.add)

            def leaky(s):
                return nc.vector.tensor_tensor(M[:, s, :], PRE[s][:, :], M[:, s, :], ALU.max)

            def finish_message(r, s):
                dve.wait_ge(B_low[s], r + 1)
                leaky(s).then_inc(B_msg[s], 1)

            def finish_sums(r, s):
                base = dve.value_load(meta[0:1, 1, bass.ds((r * SLOTS + s) * 4, 1)], min_val=0, max_val=N_NODES)
                dve.wait_ge(B_acc[s - 1], r + (2 if s else 1))
                dve.wait_ge(B_mm[s], r + 1)
                add_window(base, W1, ACC[s]).then_inc(B_acc[s], 1)

            with dve.Fori(0, ROUNDS) as r:
                for s in range(SLOTS):
                    c = r * SLOTS + s
                    dve.wait_ge(B_in[s], 48 * (r + 1))
                    nc.vector.tensor_scalar(OHT[0:W1, s, :], DB[:, s, :], pbase[0:W1, bass.ds(c, 1)], None, ALU.is_equal)
                    onehots(OH[:, s], lambda j: rel1[:, bass.ds(c * TPC + j, 1)]).then_inc(B_oh[s], 1)
                for s in range(SLOTS):
                    c = r * SLOTS + s
                    base, nx, before = load_meta(dve, 1, c)

                    def extra(k, n):
                        dve.wait_ge(B_acc[s - 2 if s >= 2 else SLOTS - 1], r + (2 if s >= 2 else 1))
                        nc.vector.tensor_scalar(relx[:, :], rel1[:, bass.ds(c * TPC, TPC)], shift[:, 1, bass.ds(k, 1)],
                                                None, ALU.subtract)
                        nc.vector.tensor_scalar(pbx[:, :], pbase[:, bass.ds(c, 1)], shift[:, 1, bass.ds(k, 1)],
                                                None, ALU.add).then_inc(Bx_rel, 1)
                        dve.wait_ge(Bx_rel, n)
                        dve.wait_ge(Bx_in, 48 * n)
                        nc.vector.tensor_scalar(OHTx[0:W1, :], DBx[:, :], pbx[0:W1, :], None, ALU.is_equal)
                        onehots(OHx, lambda j: relx[:, j:j + 1]).then_inc(Bx_oh, 1)
                        dve.wait_ge(Bx_pre, n)
                        add_u(s).then_inc(Bx_add, 1)
                        dve.wait_ge(Bx_low, n)
                        leaky(s).then_inc(Bx_msg, 1)
                        dve.wait_ge(Bx_mm, n)
                        dve.wait_ge(Bx_acc, n)
                        add_window(window_start(base, k, W1), W1, ACC[s]).then_inc(Bx_acc, 1)
                    hold(dve, B_g[s], 16 * TPC * (r + 1))
                    extra_windows(dve, nx, before, extra)
                    dve.wait_ge(Bx_acc, before + nx + 1)
                    dve.wait_ge(B_pre[s], r + 2)
                    add_u(s).then_inc(B_add[s], 1)
                    if s >= 1:
                        finish_sums(r, s - 1)
                    finish_message(r, s)
                finish_sums(r, SLOTS - 1)
            dve.wait_ge(B_acc[SLOTS - 1], ROUNDS + 1)
            dve.sem_inc(s_acc1, 1)

            with dve.Fori(0, GROUPS) as g:
                dve.wait_ge(f_z, g + 2)
                parts = ((ps[0][:, :], root[:, bass.ds(g * GW, 512)]),
                         (ps[1][:, 0:GW - 512], root[:, bass.ds(g * GW + 512, GW - 512)]))
                for product, r in parts:
                    last = nc.vector.tensor_tensor(product, r, product, ALU.add)
                last.then_inc(f_sum, 1)
                dve.wait_ge(f_low, g + 1)
                for product, r in parts:
                    last = nc.vector.tensor_tensor(r, product, r, ALU.max)
                last.then_inc(f_max, 1)

        @block.tensor
        def _(pe):
            for s in range(SLOTS):
                pe.sem_inc(A_mm[s], 1)
                pe.sem_inc(B_pre[s], 1)
            for primed in (s_y, s_h2t, s_uvr, f_z):
                pe.sem_inc(primed, 1)

            pe.wait_ge(s_const, 2)
            pe.wait_ge(s_cmin, 1)
            for h in range(2):
                for m in range(2):
                    last = nc.tensor.transpose(ps[2 * h + m][0:CH2, 0:P], cmin[:, m, h * CH2:(h + 1) * CH2], ident[:, :])
            last.then_inc(s_cminT, 1)
            pe.wait_ge(s_crep, 1)
            for h in range(2):
                for m in range(3):
                    last = nc.tensor.matmul(ps[4 + h][:, m * P:m * P + CH2], crep[:, h, m, :], ident[0:CH2, 0:CH2],
                                            start=True, stop=True)
            last.then_inc(s_cb, 1)
            pe.wait_ge(s_meta, 1)

            def segment_sums(s, onehot, rows, w):
                for j in range(TPC):
                    last = nc.tensor.matmul(ACC[s][:, 0:w], rows(j), onehot[:, j, 0:w], start=(j == 0), stop=(j == TPC - 1))
                return last

            with pe.Fori(0, ROUNDS) as r:
                for s in range(SLOTS):
                    _, nx, before = load_meta(pe, 0, r * SLOTS + s)
                    pe.wait_ge(A_acc[s], r + 1)
                    pe.wait_ge(A_g[s], 16 * TPC * (r + 1))

                    def extra(k, n):
                        pe.wait_ge(Ax_oh, n)
                        pe.wait_ge(Ax_acc, n)
                        segment_sums(s, OHx, lambda j: G[:, s, j, :], W0).then_inc(Ax_mm, 1)
                    extra_windows(pe, nx, before, extra)
                    pe.wait_ge(Ax_acc, before + nx + 1)
                    pe.wait_ge(A_oh[s], r + 1)
                    segment_sums(s, OH[:, s], lambda j: G[:, s, j, :], W0).then_inc(A_mm[s], 1)

            def y_group(g):
                pe.wait_ge(s_agg, g + 1)
                pe.wait_ge(s_x1, g + 1)
                for j in range(GT):
                    last = nc.tensor.matmul(ps[j // 4][:, (j % 4) * D:(j % 4 + 1) * D], agg[:, j * P:(j + 1) * P],
                                            w0s[:, :], start=True, stop=True)
                last.then_inc(s_y, 1)

            def transpose_group(g):
                pe.wait_ge(s_h2, g + 1)
                pe.wait_ge(s_h2T, g + 1)
                for j in range(GT):
                    last = nc.tensor.transpose(ps[2 + j // 4][:, (j % 4) * P:(j % 4 + 1) * P], h2[:, j * D:(j + 1) * D], ident[:, :])
                last.then_inc(s_h2t, 1)

            def uvr_group(g):
                pe.wait_ge(s_h2T, g + 2)
                for j in range(GT):
                    eng, semaphore = (nc.scalar, s_uv) if j in TAKERS[nc.scalar] else (nc.vector, s_root)
                    group, tile = (g, j - 4) if j >= 4 else (g - 1, 3 if j == 3 else j + 4)
                    pe.wait_ge(semaphore, taken(eng, group, tile))
                    nc.tensor.matmul(ps[4 + j % 4][:, 0:3 * D], h2T[:, j * P:(j + 1) * P],
                                     wuvr[:, :, :].rearrange("p k d -> p (k d)"), start=True, stop=True).then_inc(s_uvr, 1)

            pe.wait_ge(s_weights, 16 * (7 + SLOTS))
            y_group(0)
            with pe.Fori(0, GROUPS - 1) as g:
                transpose_group(g)
                y_group(g + 1)
                uvr_group(g)
            transpose_group(GROUPS - 1)
            uvr_group(GROUPS - 1)

            def spread_v(s, onehot_t, window):
                for j in range(TPC):
                    last = nc.tensor.matmul(PRE[s][:, j * D:(j + 1) * D], onehot_t[:, j * P:(j + 1) * P], window,
                                            start=True, stop=True)
                return last

            def message_sums(r, s):
                pe.wait_ge(B_msg[s], r + 2)
                segment_sums(s, OH[:, s], lambda j: M[:, s, j * D:(j + 1) * D], W1).then_inc(B_mm[s], 1)

            pe.wait_ge(s_uv, taken(nc.scalar, GROUPS - 1, GT - 1))
            pe.wait_ge(s_root, taken(nc.vector, GROUPS - 1, GT - 2))
            with pe.Fori(0, ROUNDS) as r:
                for s in range(SLOTS):
                    _, nx, before = load_meta(pe, 1, r * SLOTS + s)
                    pe.wait_ge(B_acc[s], r + 1)
                    pe.wait_ge(B_msg[s], r + 1)

                    def extra(k, n):
                        pe.wait_ge(Bx_acc, n)
                        pe.wait_ge(Bx_oh, n)
                        spread_v(s, OHTx, VWx[:, :]).then_inc(Bx_pre, 1)
                        pe.wait_ge(Bx_msg, n)
                        segment_sums(s, OHx, lambda j: M[:, s, j * D:(j + 1) * D], W1).then_inc(Bx_mm, 1)
                    extra_windows(pe, nx, before, extra)
                    pe.wait_ge(Bx_acc, before + nx + 1)
                    pe.wait_ge(B_in[s], 48 * (r + 1))
                    pe.wait_ge(B_oh[s], r + 2)
                    spread_v(s, OHT[:, s, :], VW[:, s, :]).then_inc(B_pre[s], 1)
                    if s >= 1:
                        message_sums(r, s - 1)
                message_sums(r, SLOTS - 1)

            with pe.Fori(0, GROUPS) as g:
                pe.wait_ge(f_agg, g + 1)
                pe.wait_ge(f_max, g + 1)
                for j in range(GT):
                    last = nc.tensor.matmul(ps[j // 4][:, (j % 4) * D:(j % 4 + 1) * D], agg[:, j * P:(j + 1) * P],
                                            wn2[:, :], start=True, stop=True)
                last.then_inc(f_z, 1)


def kernel(x, src, dst, edge_weight, L0_gnn_weight, L0_gnn_bias, L1_gnn_edge_w, L1_gnn_node_w):
    import numpy as np
    import concourse.bacc as bacc
    from concourse.bass_utils import run_bass_kernel_spmd

    pad = TILES * P - N_EDGES

    def padded(a, value):
        return np.pad(np.asarray(a), (0, pad), constant_values=value)

    def tiles(a):
        return np.ascontiguousarray(a.reshape(TILES, P).T)

    src_p, dst_p, w_p = padded(src, 0), padded(dst, N_NODES), padded(edge_weight, 0)
    arrays = {
        "in_x": np.pad(np.asarray(x), ((0, NP - N_NODES), (0, 0))),
        "in_src": tiles(src_p), "in_dst": tiles(dst_p), "in_w": tiles(w_p),
        "in_dst_row": dst_p[None, :], "in_w_row": w_p[None, :],
        "in_w0": np.asarray(L0_gnn_weight), "in_b0": np.asarray(L0_gnn_bias),
        "in_edge_w": np.asarray(L1_gnn_edge_w), "in_node_w": np.asarray(L1_gnn_node_w),
    }
    arrays = {name: np.ascontiguousarray(a) for name, a in arrays.items()}
    nc = bacc.Bacc("TRN2", target_bir_lowering=False, num_devices=1)
    args = [nc.dram_tensor(name, a.shape, mybir.dt.from_np(a.dtype), kind="ExternalInput").ap() for name, a in arrays.items()]
    out = nc.dram_tensor("out_0", (N_NODES, D), F32, kind="ExternalOutput").ap()
    gnn_kernel(nc, *args, out)
    return run_bass_kernel_spmd(nc, [arrays], core_ids=[0]).results[0]["out_0"]
```
